# Optimizing a Trainium2 kernel written in Bass

```python
import numpy as np
import jax
import jax.numpy as jnp

def _softmax(x, axis=-1):
    return jax.nn.softmax(x, axis=axis)

def _gelu(x):
    return jax.nn.gelu(x, approximate=True)

def _silu(x):
    return jax.nn.silu(x)

def _sigmoid(x):
    return jax.nn.sigmoid(x)

def _layernorm(x, axis=-1, eps=1e-05):
    m = jnp.mean(x, axis=axis, keepdims=True)
    v = jnp.var(x, axis=axis, keepdims=True)
    return (x - m) / jnp.sqrt(v + eps)

def _scatter_add(tgt, idx, src, axis=0):
    return tgt.at[idx].add(src)

def _segment_sum(src, seg, n):
    return jax.ops.segment_sum(src, seg, n)
kernel_name = 'mk_dlrm_tower_d1_rec_r8_602d09'

def setup_inputs(seed: int=0):
    np.random.seed(seed)
    _w = jnp.asarray

    def _rec_inputs():
        import jax
        import jax.numpy as jnp
        _tk = jax.random.key(seed)
        dense_ctx = jax.random.normal(jax.random.fold_in(_tk, 190), (512, 16), jnp.float32)
        ids = jnp.stack([jax.random.randint(jax.random.fold_in(_tk, 200 + f), (512,), 0, v, jnp.int32) for f, v in enumerate([125000, 1000, 12500, 12500, 1250, 12500, 12500, 12500, 1250, 12500, 12500, 12500, 1000, 1000, 1250, 1000, 12500, 1000, 1250, 1000, 1000, 1000, 1000, 1000, 1000, 1000, 1000])], axis=1)
        tbl_0 = 0.05 * jax.random.normal(jax.random.fold_in(_tk, 500 + 0), (125000, 128), jnp.float32)
        tbl_1 = 0.05 * jax.random.normal(jax.random.fold_in(_tk, 500 + 1), (1000, 128), jnp.float32)
        tbl_2 = 0.05 * jax.random.normal(jax.random.fold_in(_tk, 500 + 2), (12500, 128), jnp.float32)
        tbl_3 = 0.05 * jax.random.normal(jax.random.fold_in(_tk, 500 + 3), (12500, 128), jnp.float32)
        tbl_4 = 0.05 * jax.random.normal(jax.random.fold_in(_tk, 500 + 4), (1250, 128), jnp.float32)
        tbl_5 = 0.05 * jax.random.normal(jax.random.fold_in(_tk, 500 + 5), (12500, 128), jnp.float32)
        tbl_6 = 0.05 * jax.random.normal(jax.random.fold_in(_tk, 500 + 6), (12500, 128), jnp.float32)
        tbl_7 = 0.05 * jax.random.normal(jax.random.fold_in(_tk, 500 + 7), (12500, 128), jnp.float32)
        tbl_8 = 0.05 * jax.random.normal(jax.random.fold_in(_tk, 500 + 8), (1250, 128), jnp.float32)
        tbl_9 = 0.05 * jax.random.normal(jax.random.fold_in(_tk, 500 + 9), (12500, 128), jnp.float32)
        tbl_10 = 0.05 * jax.random.normal(jax.random.fold_in(_tk, 500 + 10), (12500, 128), jnp.float32)
        tbl_11 = 0.05 * jax.random.normal(jax.random.fold_in(_tk, 500 + 11), (12500, 128), jnp.float32)
        tbl_12 = 0.05 * jax.random.normal(jax.random.fold_in(_tk, 500 + 12), (1000, 128), jnp.float32)
        tbl_13 = 0.05 * jax.random.normal(jax.random.fold_in(_tk, 500 + 13), (1000, 128), jnp.float32)
        tbl_14 = 0.05 * jax.random.normal(jax.random.fold_in(_tk, 500 + 14), (1250, 128), jnp.float32)
        tbl_15 = 0.05 * jax.random.normal(jax.random.fold_in(_tk, 500 + 15), (1000, 128), jnp.float32)
        tbl_16 = 0.05 * jax.random.normal(jax.random.fold_in(_tk, 500 + 16), (12500, 128), jnp.float32)
        tbl_17 = 0.05 * jax.random.normal(jax.random.fold_in(_tk, 500 + 17), (1000, 128), jnp.float32)
        tbl_18 = 0.05 * jax.random.normal(jax.random.fold_in(_tk, 500 + 18), (1250, 128), jnp.float32)
        tbl_19 = 0.05 * jax.random.normal(jax.random.fold_in(_tk, 500 + 19), (1000, 128), jnp.float32)
        tbl_20 = 0.05 * jax.random.normal(jax.random.fold_in(_tk, 500 + 20), (1000, 128), jnp.float32)
        tbl_21 = 0.05 * jax.random.normal(jax.random.fold_in(_tk, 500 + 21), (1000, 128), jnp.float32)
        tbl_22 = 0.05 * jax.random.normal(jax.random.fold_in(_tk, 500 + 22), (1000, 128), jnp.float32)
        tbl_23 = 0.05 * jax.random.normal(jax.random.fold_in(_tk, 500 + 23), (1000, 128), jnp.float32)
        tbl_24 = 0.05 * jax.random.normal(jax.random.fold_in(_tk, 500 + 24), (1000, 128), jnp.float32)
        tbl_25 = 0.05 * jax.random.normal(jax.random.fold_in(_tk, 500 + 25), (1000, 128), jnp.float32)
        tbl_26 = 0.05 * jax.random.normal(jax.random.fold_in(_tk, 500 + 26), (1000, 128), jnp.float32)
        _rk = jax.random.fold_in(_tk, 7)
        W_top1 = 0.0521996 * jax.random.normal(jax.random.fold_in(_tk, 801), (367, 512), jnp.float32)
        W_top2 = 0.0441942 * jax.random.normal(jax.random.fold_in(_tk, 802), (512, 256), jnp.float32)
        W_top3 = 0.0625 * jax.random.normal(jax.random.fold_in(_tk, 803), (256, 1), jnp.float32)
        b_top1 = jnp.zeros((512,), jnp.float32)
        b_top2 = jnp.zeros((256,), jnp.float32)
        return (dense_ctx, ids, tbl_0, tbl_1, tbl_2, tbl_3, tbl_4, tbl_5, tbl_6, tbl_7, tbl_8, tbl_9, tbl_10, tbl_11, tbl_12, tbl_13, tbl_14, tbl_15, tbl_16, tbl_17, tbl_18, tbl_19, tbl_20, tbl_21, tbl_22, tbl_23, tbl_24, tbl_25, tbl_26, W_top1, b_top1, W_top2, b_top2, W_top3)
    dense_ctx, ids, tbl_0, tbl_1, tbl_2, tbl_3, tbl_4, tbl_5, tbl_6, tbl_7, tbl_8, tbl_9, tbl_10, tbl_11, tbl_12, tbl_13, tbl_14, tbl_15, tbl_16, tbl_17, tbl_18, tbl_19, tbl_20, tbl_21, tbl_22, tbl_23, tbl_24, tbl_25, tbl_26, W_top1, b_top1, W_top2, b_top2, W_top3 = _rec_inputs()

    def _L0_rec_setup():
        import jax, jax.numpy as jnp
        import numpy as np

        def _tri_indices(num_feas):
            return np.array([i * num_feas + j for j in range(1, num_feas) for i in range(j)], dtype=np.int32)
        key = jax.random.key(seed)
        batch, num_feas, embed_dim = (2048, 27, 128)
        inputs = jax.random.normal(key, (batch, num_feas, embed_dim), dtype=jnp.float32)
        return {'inputs': inputs, 'num_feas': num_feas}
    _L0_rec_all = _L0_rec_setup()
    _L0_rec_in = {k: v for k, v in _L0_rec_all.items() if k in ()}
    del _L0_rec_all
    return {'dense_ctx': dense_ctx, 'ids': ids, 'tbl_0': tbl_0, 'tbl_1': tbl_1, 'tbl_2': tbl_2, 'tbl_3': tbl_3, 'tbl_4': tbl_4, 'tbl_5': tbl_5, 'tbl_6': tbl_6, 'tbl_7': tbl_7, 'tbl_8': tbl_8, 'tbl_9': tbl_9, 'tbl_10': tbl_10, 'tbl_11': tbl_11, 'tbl_12': tbl_12, 'tbl_13': tbl_13, 'tbl_14': tbl_14, 'tbl_15': tbl_15, 'tbl_16': tbl_16, 'tbl_17': tbl_17, 'tbl_18': tbl_18, 'tbl_19': tbl_19, 'tbl_20': tbl_20, 'tbl_21': tbl_21, 'tbl_22': tbl_22, 'tbl_23': tbl_23, 'tbl_24': tbl_24, 'tbl_25': tbl_25, 'tbl_26': tbl_26, 'W_top1': W_top1, 'b_top1': b_top1, 'W_top2': W_top2, 'b_top2': b_top2, 'W_top3': W_top3}

def reference(dense_ctx, ids, tbl_0, tbl_1, tbl_2, tbl_3, tbl_4, tbl_5, tbl_6, tbl_7, tbl_8, tbl_9, tbl_10, tbl_11, tbl_12, tbl_13, tbl_14, tbl_15, tbl_16, tbl_17, tbl_18, tbl_19, tbl_20, tbl_21, tbl_22, tbl_23, tbl_24, tbl_25, tbl_26, W_top1, b_top1, W_top2, b_top2, W_top3):
    import jax
    import jax.numpy as jnp

    def _L0_rec_ref(inputs, num_feas):
        import jax, jax.numpy as jnp
        import numpy as np

        def _tri_indices(num_feas):
            return np.array([i * num_feas + j for j in range(1, num_feas) for i in range(j)], dtype=np.int32)
        dot = jnp.einsum('bnd,bmd->bnm', inputs, inputs)
        idx = jnp.asarray(_tri_indices(num_feas))
        flat = dot.reshape(inputs.shape[0], num_feas * num_feas)
        return flat[:, idx]
    e = jnp.stack([tbl_0[ids[:, 0]], tbl_1[ids[:, 1]], tbl_2[ids[:, 2]], tbl_3[ids[:, 3]], tbl_4[ids[:, 4]], tbl_5[ids[:, 5]], tbl_6[ids[:, 6]], tbl_7[ids[:, 7]], tbl_8[ids[:, 8]], tbl_9[ids[:, 9]], tbl_10[ids[:, 10]], tbl_11[ids[:, 11]], tbl_12[ids[:, 12]], tbl_13[ids[:, 13]], tbl_14[ids[:, 14]], tbl_15[ids[:, 15]], tbl_16[ids[:, 16]], tbl_17[ids[:, 17]], tbl_18[ids[:, 18]], tbl_19[ids[:, 19]], tbl_20[ids[:, 20]], tbl_21[ids[:, 21]], tbl_22[ids[:, 22]], tbl_23[ids[:, 23]], tbl_24[ids[:, 24]], tbl_25[ids[:, 25]], tbl_26[ids[:, 26]]], axis=1)
    z = _L0_rec_ref(e, 27)
    z = z.reshape(z.shape[0], -1)
    h = jnp.concatenate([z, dense_ctx], axis=1)
    h = jnp.maximum(h @ W_top1 + b_top1, 0.0)
    h = jnp.maximum(h @ W_top2 + b_top2, 0.0)
    y = h @ W_top3
    return y

_drawn_inputs = setup_inputs


def setup_inputs(seed=0):
    import zlib

    import numpy as np

    out = dict(_drawn_inputs(seed))
    spreads = {'b_top1': (0.0, 0.1), 'b_top2': (0.0, 0.1)}
    factors = {}
    for name, (base, spread) in spreads.items():
        noise = np.random.default_rng([zlib.crc32(name.encode()), seed]).standard_normal(out[name].shape)
        drawn = base * np.exp(spread * noise) if base else spread * noise
        out[name] = jnp.asarray(drawn.astype(out[name].dtype))
    for name, factor in factors.items():
        out[name] = (out[name] * factor).astype(out[name].dtype)
    return out
```

```python
from contextlib import ExitStack

import numpy as np

import concourse.bass as bass
from concourse import mybir

P = 128
T = 4
B = T * P
F = 27
SLOTS = 32
DENSE = 16
H1, H2 = 512, 256
HOT = 9
CH = 8
HR = 125
PER = 4
GROUPS = P // 4
WG = [12, 12, 8]
NJ = 4
KT = 7

V = [125000, 1000, 12500, 12500, 1250, 12500, 12500, 12500, 1250, 12500, 12500, 12500, 1000,
     1000, 1250, 1000, 12500, 1000, 1250, 1000, 1000, 1000, 1000, 1000, 1000, 1000, 1000]
HOT_F = [f for f in range(F) if V[f] == CH * HR][:HOT]
GAT_F = [f for f in range(F) if f not in HOT_F]
ORDER = GAT_F + HOT_F
NG = len(GAT_F)
GG = [list(range(a, min(a + PER, NG))) for a in range(0, NG, PER)]

F32 = mybir.dt.float32
F32R = mybir.dt.float32r
I32 = mybir.dt.int32
U32 = mybir.dt.uint32
ALU = mybir.AluOpType
ACT = mybir.ActivationFunctionType


def plan():
    steps = []
    tr = [(t, g) for t in range(T) for g in range(len(GG))]
    for k in range(HOT):
        steps.append(("hot", k, 0))
        if k >= 1 and tr:
            steps.append(("turn",) + tr.pop(0))
    for t in range(T):
        while tr and tr[0][0] <= t:
            steps.append(("turn",) + tr.pop(0))
        for w in range(len(WG)):
            steps.append(("dots", t, w))
            if w < len(WG) - 1 and tr and t < T - 1:
                pass
        if tr:
            steps.append(("turn",) + tr.pop(0))
        steps.append(("mlp", t, 0))
    return steps


def build(nc, ids, ids_hot, dense, tables, w1, b1, w2, b2, w3, consts, out):
    steps = plan()
    turns = [(t, g) for kind, t, g in steps if kind == "turn"]
    windows = [(t, w) for t in range(T) for w in range(len(WG))]

    with ExitStack() as ctx:
        def sb(name, shape, dt=F32):
            return ctx.enter_context(nc.sbuf_tensor(name, shape, dt))

        def sem(name):
            return ctx.enter_context(nc.semaphore(name))

        ids_sb = sb("ids_sb", [P, T * F], I32)
        csb = sb("csb", [P, P + CH])
        idsb = sb("idsb", [P, 3, B], I32)
        raw = sb("raw", [P, 2, CH, P])
        hi = sb("hi", [P, 2, CH, P], F32R)
        lo = sb("lo", [P, 2, CH, P], F32R)
        onehot = sb("onehot", [P, 3, CH // 2, B], F32R)
        E = sb("E", [P, 2, NG, P])
        eT = sb("eT", [P, B, SLOTS])
        G = sb("G", [P, T, KT, P])
        w1_sb = sb("w1_sb", [P, KT, H1])
        w2_sb = sb("w2_sb", [P, H1 // P, H2])
        wb = sb("wb", [P, 8])
        dn = sb("dn", [P, T, DENSE])
        h1 = sb("h1", [P, H1 // P, P])
        h2 = sb("h2", [P, H2 // P, P])
        y = sb("y", [P, T])
        ident = csb[:, 0:P]
        ps = ctx.enter_context(nc.psum_tensor("ps", [P, 8, 512], F32))
        TURN, MLP = 6, 7

        ids_in, const_in, dense_in, w_in = sem("ids_in"), sem("const_in"), sem("dense_in"), sem("w_in")
        idsb_in = [sem(f"idsb_in{k}") for k in range(HOT)]
        raw_in = [sem(f"raw_in{k}") for k in range(HOT)]
        gathered = {(t, g): sem(f"gathered{t}_{g}") for t in range(T) for g in range(len(GG))}
        padded, hi_done, lo_done = sem("padded"), sem("hi_done"), sem("lo_done")
        onehot_done, onehot_used = sem("onehot_done"), sem("onehot_used")
        hot_out = sem("hot_out")
        turn_done, turn_out = sem("turn_done"), sem("turn_out")
        dense_turned, dense_out = sem("dense_turned"), sem("dense_out")
        dots_done, dots_out_v, dots_out_s = sem("dots_done"), sem("dots_out_v"), sem("dots_out_s")
        l1_done, l1_out, l2_done, l2_out = sem("l1_done"), sem("l1_out"), sem("l2_done"), sem("l2_out")
        l3_done, l3_out, stored = sem("l3_done"), sem("l3_out"), sem("stored")
        block = ctx.enter_context(nc.Block())

        def window(t, w):
            return 3 * ((len(WG) * t + w) % 2), WG[w], sum(WG[:w])

        def evacuate(copy, quads, t, w):
            bank, n, g0 = window(t, w)
            for s in quads:
                for m in range(NJ):
                    k = len(range(m, F, NJ))
                    src = ps[32 * s:32 * s + 32, bank:bank + 3, :].rearrange("p k (g c) -> p (k g) c", c=P)
                    src = src[:, 0:n, F * s + m:F * s + F:NJ].rearrange("p g k -> p k g")
                    dst = G[32 * m:32 * m + 32, t, 0:k, 4 * g0 + s:4 * (g0 + n):4]
                    last = copy(dst, src)
            return last

        @block.sync
        def _(sp):
            sp.dma_start(ids_sb[:, :], ids).then_inc(ids_in, 16)
            sp.dma_start(csb[:, :], consts).then_inc(const_in, 16)
            for k in range(HOT):
                if k >= 3:
                    sp.wait_ge(onehot_done, 2 * (k - 2))
                sp.dma_start(idsb[0:HR, k % 3, :],
                             ids_hot[k:k + 1, :].to_broadcast([HR, B])).then_inc(idsb_in[k], 16)
                if k >= 2:
                    sp.wait_ge(lo_done, k - 1)
                sp.dma_start(raw[0:HR, k % 2, :, :],
                             tables[HOT_F[k]].rearrange("(p c) d -> p c d", c=CH)).then_inc(raw_in[k], 16)
                if k == 2:
                    sp.dma_start(dn[:, :, :], dense.rearrange("(p t) f -> p t f", t=T)).then_inc(dense_in, 16)
            sp.dma_start(w1_sb[:, :, :], w1).then_inc(w_in, 16)
            sp.dma_start(w2_sb[:, :, :], w2.rearrange("(k p) n -> p k n", p=P)).then_inc(w_in, 16)
            sp.dma_start(wb[:, 0:4], b1).then_inc(w_in, 16)
            sp.dma_start(wb[:, 4:6], b2).then_inc(w_in, 16)
            sp.dma_start(wb[:, 6:8], w3).then_inc(w_in, 16)
            sp.wait_ge(l3_out, T)
            sp.dma_start(out.rearrange("(p t) f -> p (t f)", t=T), y[:, :]).then_inc(stored, 16)
            sp.wait_ge(stored, 16)

        @block.gpsimd
        def _(pool):
            pool.wait_ge(ids_in, 16)
            for t in range(T):
                for g, slots in enumerate(GG):
                    if t >= 2:
                        pool.wait_ge(turn_done, turns.index((t - 2, g)) + 1)
                    for slot in slots:
                        f = ORDER[slot]
                        pool.indirect_dma_start(
                            out=E[:, t % 2, slot, :], out_offset=None, in_=tables[f],
                            in_offset=bass.IndirectOffsetOnAxis(
                                ap=ids_sb[:, t * F + f:t * F + f + 1].bitcast(U32), axis=0),
                        ).then_inc(gathered[t, g], 16)

        @block.tensor
        def _(pe):
            pe.wait_ge(const_in, 16)
            dense_at = 1
            for n, (kind, a, b) in enumerate(steps):
                if n == dense_at:
                    pe.wait_ge(dense_in, 16)
                    for t in range(T):
                        mm = pe.transpose(ps[0:DENSE, TURN, t * P:(t + 1) * P], dn[:, t, :], ident)
                    mm.then_inc(dense_turned, 1)
                if kind == "hot":
                    k = a
                    if k >= 2:
                        pe.wait_ge(hot_out, k - 1)
                    pe.wait_ge(hi_done, k + 1)
                    pe.wait_ge(lo_done, k + 1)
                    for c in range(CH):
                        if c % 4 == 0:
                            pe.wait_ge(onehot_done, 2 * k + c // 4 + 1)
                        cols = onehot[0:HR, (2 * k + c // 4) % 3, c % 4, :]
                        pe.matmul(ps[:, k % 2, :], hi[0:HR, k % 2, c, :], cols, start=(c == 0), stop=False)
                        mm = pe.matmul(ps[:, k % 2, :], lo[0:HR, k % 2, c, :], cols,
                                       start=False, stop=(c == CH - 1))
                        if c == 3:
                            mm.then_inc(onehot_used, 1)
                    mm.then_inc(onehot_used, 1)
                elif kind == "turn":
                    i = turns.index((a, b))
                    pe.wait_ge(gathered[a, b], 16 * len(GG[b]))
                    if i == 0:
                        pe.wait_ge(dense_out, 1)
                    else:
                        pe.wait_ge(turn_out, i)
                    for q, slot in enumerate(GG[b]):
                        mm = pe.transpose(ps[:, TURN, q * P:(q + 1) * P], E[:, a % 2, slot, :], ident)
                    mm.then_inc(turn_done, 1)
                elif kind == "dots":
                    bank, ng, g0 = window(a, b)
                    i = windows.index((a, b))
                    if b == 0:
                        pe.wait_ge(padded, 1)
                        pe.wait_ge(hot_out, HOT)
                        pe.wait_ge(turn_out, turns.index((a, len(GG) - 1)) + 1)
                    if i >= 2:
                        pe.wait_ge(dots_out_v, i - 1)
                        pe.wait_ge(dots_out_s, i - 1)
                    for g in range(ng):
                        c0 = a * P + 4 * (g0 + g)
                        mm = pe.matmul(ps[:, bank + g // 4, (g % 4) * P:(g % 4) * P + 4 * F],
                                       eT[:, c0:c0 + 4, :].rearrange("p s f -> p (s f)"),
                                       eT[:, c0:c0 + 4, 0:F], start=True, stop=True)
                    mm.then_inc(dots_done, 1)
                else:
                    t = a
                    if t == 0:
                        pe.wait_ge(w_in, 80)
                        pe.wait_ge(dense_out, 1)
                    else:
                        pe.wait_ge(l3_out, t)
                    pe.wait_ge(dots_out_v, len(WG) * (t + 1))
                    pe.wait_ge(dots_out_s, len(WG) * (t + 1))
                    for n1 in range(H1 // P):
                        for k in range(KT):
                            r = P if k < KT - 1 else 96 + DENSE
                            mm = pe.matmul(ps[:, MLP, n1 * P:(n1 + 1) * P], w1_sb[0:r, k, n1 * P:(n1 + 1) * P],
                                           G[0:r, t, k, :], start=(k == 0), stop=(k == KT - 1))
                    mm.then_inc(l1_done, 1)
                    pe.wait_ge(l1_out, t + 1)
                    for n2 in range(H2 // P):
                        for k in range(H1 // P):
                            mm = pe.matmul(ps[:, MLP, n2 * P:(n2 + 1) * P], w2_sb[:, k, n2 * P:(n2 + 1) * P],
                                           h1[:, k, :], start=(k == 0), stop=(k == H1 // P - 1))
                    mm.then_inc(l2_done, 1)
                    pe.wait_ge(l2_out, t + 1)
                    for k in range(H2 // P):
                        mm = pe.matmul(ps[:, MLP, 0:1], h2[:, k, :], wb[:, 6 + k:7 + k],
                                       start=(k == 0), stop=(k == H2 // P - 1))
                    mm.then_inc(l3_done, 1)

        @block.vector
        def _(dve):
            dve.memset(eT[:, :, F:SLOTS], 0.0).then_inc(padded, 1)

            def prepare(k):
                for half in range(2):
                    i = 2 * k + half
                    if half == 0:
                        dve.wait_ge(idsb_in[k], 16)
                        if k == 0:
                            dve.wait_ge(const_in, 16)
                    if i >= 3:
                        dve.wait_ge(onehot_used, i - 2)
                    for c in range(CH // 2):
                        j = half * CH // 2 + c
                        op = dve.tensor_scalar(onehot[0:HR, i % 3, c, :], idsb[0:HR, k % 3, :],
                                               csb[0:HR, P + j:P + j + 1], None, ALU.is_equal)
                    op.then_inc(onehot_done, 1)
                    if half == 0:
                        dve.wait_ge(hi_done, k + 1)
                        if k >= 2:
                            dve.wait_ge(onehot_used, 2 * (k - 1))
                        dve.tensor_tensor(lo[0:HR, k % 2, :, :], raw[0:HR, k % 2, :, :],
                                          hi[0:HR, k % 2, :, :].bitcast(F32), ALU.subtract).then_inc(lo_done, 1)

            prepare(0)
            for kind, a, b in steps:
                if kind == "hot" and a + 1 < HOT:
                    prepare(a + 1)
                elif kind == "dots":
                    dve.wait_ge(dots_done, windows.index((a, b)) + 1)
                    evacuate(lambda d, s: dve.tensor_copy(d, s), (0, 1), a, b).then_inc(dots_out_v, 1)

        @block.scalar
        def _(act):
            def split(k):
                act.wait_ge(raw_in[k], 16)
                if k >= 2:
                    act.wait_ge(onehot_used, 2 * (k - 1))
                act.copy(hi[0:HR, k % 2, :, :], raw[0:HR, k % 2, :, :]).then_inc(hi_done, 1)

            split(0)
            for n, (kind, a, b) in enumerate(steps):
                if n == 1:
                    act.wait_ge(dense_turned, 1)
                    act.copy(G[96:96 + DENSE, :, KT - 1, :],
                             ps[0:DENSE, TURN, :].rearrange("p (t b) -> p t b", t=T)).then_inc(dense_out, 1)
                if kind == "hot":
                    if a + 1 < HOT:
                        split(a + 1)
                    act.wait_ge(onehot_used, 2 * (a + 1))
                    act.copy(eT[:, :, NG + a], ps[:, a % 2, :]).then_inc(hot_out, 1)
                elif kind == "turn":
                    s0, ns = GG[b][0], len(GG[b])
                    act.wait_ge(turn_done, turns.index((a, b)) + 1)
                    act.copy(eT[:, a * P:(a + 1) * P, s0:s0 + ns],
                             ps[:, TURN, 0:ns * P].rearrange("p (f b) -> p b f", f=ns)).then_inc(turn_out, 1)
                elif kind == "dots":
                    act.wait_ge(dots_done, windows.index((a, b)) + 1)
                    evacuate(lambda d, s: act.copy(d, s), (2, 3), a, b).then_inc(dots_out_s, 1)
                else:
                    act.wait_ge(l1_done, a + 1)
                    for k in range(H1 // P):
                        op = act.activation(h1[:, k, :], ps[:, MLP, k * P:(k + 1) * P], ACT.Relu,
                                            bias=wb[:, k:k + 1])
                    op.then_inc(l1_out, 1)
                    act.wait_ge(l2_done, a + 1)
                    for k in range(H2 // P):
                        op = act.activation(h2[:, k, :], ps[:, MLP, k * P:(k + 1) * P], ACT.Relu,
                                            bias=wb[:, 4 + k:5 + k])
                    op.then_inc(l2_out, 1)
                    act.wait_ge(l3_done, a + 1)
                    act.copy(y[:, a:a + 1], ps[:, MLP, 0:1]).then_inc(l3_out, 1)


def first_layer_rows():
    rows = np.full((P, KT), -1)
    for j in range(F):
        for i in range(j):
            a, b = sorted((ORDER[i], ORDER[j]))
            rows[32 * (j % NJ) + i, j // NJ] = b * (b - 1) // 2 + a
    for d in range(DENSE):
        rows[96 + d, KT - 1] = F * (F - 1) // 2 + d
    return rows


def kernel(**inputs):
    import concourse.bacc as bacc
    from concourse.bass_utils import run_bass_kernel_spmd

    W = np.asarray(inputs["W_top1"])
    rows = first_layer_rows()
    w1 = np.zeros((P, KT, H1), W.dtype)
    w1[rows >= 0] = W[rows[rows >= 0]]
    ids = np.asarray(inputs["ids"])
    consts = np.concatenate([np.eye(P), CH * np.arange(P)[:, None] + np.arange(CH)], 1).astype(np.float32)
    arrays = {
        "ids": ids.reshape(P, T * F),
        "ids_hot": ids.reshape(P, T, F)[:, :, HOT_F].transpose(2, 1, 0).reshape(HOT, B),
        "dense": inputs["dense_ctx"],
        "w1": w1,
        "b1": np.asarray(inputs["b_top1"]).reshape(H1 // P, P).T,
        "w2": inputs["W_top2"],
        "b2": np.asarray(inputs["b_top2"]).reshape(H2 // P, P).T,
        "w3": np.asarray(inputs["W_top3"]).reshape(H2 // P, P).T,
        "consts": consts,
    }
    for f in range(F):
        arrays[f"tbl_{f}"] = inputs[f"tbl_{f}"]
    nc = bacc.Bacc("TRN2", target_bir_lowering=False, num_devices=1)
    aps = {}
    for name in arrays:
        a = arrays[name] = np.ascontiguousarray(arrays[name])
        aps[name] = nc.dram_tensor(f"in_{name}", a.shape, mybir.dt.from_np(a.dtype), kind="ExternalInput").ap()
    out = nc.dram_tensor("out", (B, 1), F32, kind="ExternalOutput").ap()
    build(nc, aps["ids"], aps["ids_hot"], aps["dense"], [aps[f"tbl_{f}"] for f in range(F)], aps["w1"],
          aps["b1"], aps["w2"], aps["b2"], aps["w3"], aps["consts"], out)
    r = run_bass_kernel_spmd(nc, [{f"in_{n}": a for n, a in arrays.items()}], core_ids=[0])
    return r.results[0]["out"]
```

```python
from contextlib import ExitStack

import numpy as np

import concourse.bass as bass
from concourse import mybir

P = 128
T = 4
B = T * P
F = 27
PAIRED = 24
SLOTS = 32
DENSE = 16
H1, H2 = 512, 256
HOT = 9
CH = 8
HR = 125
BATCH = 2
RING = 5
WARM = 4
RAWS = 4
SPLITS = 2 * BATCH
PER = 4
WG = [12, 12, 8]
W = len(WG)
PITCH = 128
KT = 4
N1, N2 = H1 // P, H2 // P

V = [125000, 1000, 12500, 12500, 1250, 12500, 12500, 12500, 1250, 12500, 12500, 12500, 1000,
     1000, 1250, 1000, 12500, 1000, 1250, 1000, 1000, 1000, 1000, 1000, 1000, 1000, 1000]
HOT_F = [f for f in range(F) if V[f] == CH * HR][:HOT]
GAT_F = [f for f in range(F) if f not in HOT_F]
SINGLE = F - PAIRED
ORDER = GAT_F + HOT_F
NG = len(GAT_F)
GG = [list(range(a, min(a + PER, NG))) for a in range(0, NG, PER)]
BATCHES = [list(range(a, min(a + BATCH, HOT))) for a in range(0, HOT, BATCH)]

F32 = mybir.dt.float32
F32R = mybir.dt.float32r
I32 = mybir.dt.int32
U32 = mybir.dt.uint32
ALU = mybir.AluOpType
ACT = mybir.ActivationFunctionType


def parts(k):
    return [(0, CH // 2), (CH // 2, CH)] if k < BATCH else [(0, CH)]


def pieces(k, c):
    if k < BATCH:
        return (c // (CH // 2)) * len(BATCHES[0]) + k + 1
    return 2 * len(BATCHES[0]) + k - len(BATCHES[0]) + 1


def loads(b):
    return [(k,) + parts(k)[i] for i in range(len(parts(BATCHES[b][0]))) for k in BATCHES[b]]


def plan():
    cost = {"turn": 0.45, "l1": 3.5, "l2": 1.8, "l3": 0.5}
    steps = []
    turns = [(t, g) for t in range(T) for g in range(len(GG))]
    arrival, now = {}, 8.0
    for t, g in turns:
        now += 1.04 * len(GG[g])
        arrival[t, g] = now
    now = 6.5

    def add(kind, a, b):
        nonlocal now
        if kind == "turn":
            now = max(now, arrival[a, b])
        steps.append((kind, a, b))
        now += (1.75 * len(BATCHES[a]) if kind == "hot" else 0.21 * WG[b] if kind == "dots"
                else cost[kind])

    def main(kind, a, b):
        add(kind, a, b)
        if turns and arrival[turns[0]] < now:
            add("turn", *turns.pop(0))

    for b in range(len(BATCHES)):
        for half in range(2):
            main("hot", b, half)
    for t in range(T):
        layers = [(x, t - 1, 0) for x in ("l1", "l2", "l3")] if t else []
        while turns and turns[0][0] <= t:
            behind = arrival[turns[0]] <= now
            if behind or not layers:
                add("turn", *turns.pop(0))
            if layers and not (behind and (not turns or turns[0][0] > t)):
                add(*layers.pop(0))
        windows = [("dots", t, w) for w in range(W)]
        if t == T - 1:
            return steps + windows + layers + [(x, t, 0) for x in ("l1", "l2", "l3")]
        while windows or layers:
            for x in windows[:1] + layers[:1]:
                main(*x)
            windows, layers = windows[1:], layers[1:]


def build(nc, ids, ids_hot, dense, tables, w1, b1, w2, b2, w3, consts, take_c, out):
    steps = plan()
    turns = [(t, g) for kind, t, g in steps if kind == "turn"]
    dots = [(t, w) for kind, t, w in steps if kind == "dots"]

    with ExitStack() as ctx:
        def sb(name, shape, dt=F32):
            return ctx.enter_context(nc.sbuf_tensor(name, shape, dt))

        def sem(name):
            return ctx.enter_context(nc.semaphore(name))

        ids_sb = sb("ids_sb", [P, T * F], I32)
        csb = sb("csb", [P, P + CH])
        mask = sb("mask", [P, KT - 1], I32)
        warm = sb("warm", [P, 512])
        idsb = sb("idsb", [P, 2, BATCH * B], I32)
        raw = sb("raw", [P, RAWS, CH, P])
        hi = sb("hi", [P, SPLITS, CH, P], F32R)
        lo = sb("lo", [P, SPLITS, CH, P], F32R)
        onehot = sb("onehot", [P, RING, BATCH * B], F32R)
        E = sb("E", [P, 2, len(GAT_F), P])
        eT = sb("eT", [P, B, SLOTS])
        G = sb("G", [P, T, KT, P])
        w1_sb = sb("w1_sb", [P, KT, H1])
        w2_sb = sb("w2_sb", [P, N1, H2])
        wb = sb("wb", [P, N1 + 2 * N2])
        dn = sb("dn", [P, T, DENSE])
        h1 = sb("h1", [P, 2, N1, P])
        h2 = sb("h2", [P, 2, N2, P])
        y = sb("y", [P, T])
        ident = csb[:, 0:P]
        ps = ctx.enter_context(nc.psum_tensor("ps", [P, 8, 512], F32))
        TURN, MLP = 6, 7

        ids_in, const_in, dense_in, w_in = sem("ids_in"), sem("const_in"), sem("dense_in"), sem("w_in")
        idsb_in = [sem(f"idsb_in{b}") for b in range(len(BATCHES))]
        piece_in = [sem(f"piece_in{i}") for i in range(sum(len(loads(b)) for b in range(len(BATCHES))))]
        gathered = {(t, g): sem(f"gathered{t}_{g}") for t in range(T) for g in range(len(GG))}
        warm_set, pads_set = sem("warm_set"), sem("pads_set")
        hi_done, lo_done = sem("hi_done"), sem("lo_done")
        onehot_done, onehot_used, hot_out = sem("onehot_done"), sem("onehot_used"), sem("hot_out")
        turn_done, turn_out = sem("turn_done"), sem("turn_out")
        dense_turned, dense_out = sem("dense_turned"), sem("dense_out")
        dots_done, base_out, dots_out = sem("dots_done"), sem("base_out"), sem("dots_out")
        l1_done, l1_out_s, l1_out_v = sem("l1_done"), sem("l1_out_s"), sem("l1_out_v")
        l2_done, l2_out_s, l2_out_v = sem("l2_done"), sem("l2_out_s"), sem("l2_out_v")
        l3_done, l3_out, stored = sem("l3_done"), sem("l3_out"), sem("stored")
        block = ctx.enter_context(nc.Block())

        def own(i, s, first, k):
            w = dots[i][1]
            ng, g0 = WG[w], sum(WG[:w])
            src = ps[32 * s:32 * s + 32, 3 * (i % 2):3 * (i % 2) + 3, :].rearrange("p k c -> p (k c)")
            src = src[:, 0:ng * PITCH].rearrange("p (g c) -> p g c", c=PITCH)
            a = s * F + first
            src = src[:, :, a:a + 4 * (k - 1) + 1:4].rearrange("p g k -> p k g")
            return src, slice(4 * g0 + s, 4 * (g0 + ng), 4), ng

        def l1_bank(t, n):
            return n // 2 if t == T - 1 else MLP

        def l2_bank(t, n):
            return (2, TURN)[n] if t == T - 1 else MLP

        def l3_bank(t):
            return 0 if t == T - 1 else MLP

        @block.sync
        def _(sp):
            sp.dma_start(ids_sb[:, :], ids).then_inc(ids_in, 16)
            i = 0
            for b, ks in enumerate(BATCHES):
                def ids_of_batch():
                    if b >= 2:
                        sp.wait_ge(onehot_done, CH * (b - 1))
                    sp.dma_start(idsb[0:HR, b % 2, 0:len(ks) * B],
                                 ids_hot[:, ks[0] * B:(ks[-1] + 1) * B].to_broadcast([HR, len(ks) * B])
                                 ).then_inc(idsb_in[b], 16)

                if b == 1:
                    ids_of_batch()
                for k, c0, c1 in loads(b):
                    if k >= RAWS:
                        sp.wait_ge(lo_done, pieces(k - RAWS, CH - 1))
                    sp.dma_start(raw[0:HR, k % RAWS, c0:c1, :],
                                 tables[HOT_F[k]].rearrange("(p c) d -> p c d", c=CH)[:, c0:c1, :]
                                 ).then_inc(piece_in[i], 16)
                    i += 1
                    if i == 1:
                        ids_of_batch()
                        sp.dma_start(csb[:, :], consts).then_inc(const_in, 16)
                if b == 0:
                    sp.dma_start(dn[:, :, :], dense.rearrange("(p t) f -> p t f", t=T)).then_inc(dense_in, 16)
                if b >= 2:
                    ids_of_batch()
                if b == 2:
                    sp.dma_start(w1_sb[:, :, :], w1).then_inc(w_in, 16)
                    sp.dma_start(w2_sb[:, :, :], w2.rearrange("(k p) n -> p k n", p=P)).then_inc(w_in, 16)
                    sp.dma_start(wb[:, 0:N1], b1).then_inc(w_in, 16)
                    sp.dma_start(wb[:, N1:N1 + N2], b2).then_inc(w_in, 16)
                    sp.dma_start(wb[:, N1 + N2:], w3).then_inc(w_in, 16)
                    sp.dma_start(mask[:, :], take_c).then_inc(w_in, 16)
            sp.wait_ge(l3_out, T)
            sp.dma_start(out.rearrange("(p t) f -> p (t f)", t=T), y[:, :]).then_inc(stored, 16)
            sp.wait_ge(stored, 16)

        @block.gpsimd
        def _(pool):
            pool.memset(warm[:, :], 0.0).then_inc(warm_set, 1)
            pool.wait_ge(ids_in, 16)
            for t in range(T):
                for g, slots in enumerate(GG):
                    if t >= 2:
                        pool.wait_ge(turn_done, turns.index((t - 2, g)) + 1)
                    for slot in slots:
                        f = ORDER[slot]
                        pool.indirect_dma_start(
                            out=E[:, t % 2, GAT_F.index(f), :], out_offset=None, in_=tables[f],
                            in_offset=bass.IndirectOffsetOnAxis(
                                ap=ids_sb[:, t * F + f:t * F + f + 1].bitcast(U32), axis=0),
                        ).then_inc(gathered[t, g], 16)

        @block.tensor
        def _(pe):
            def hot(b, half):
                if half == 0 and b >= 2:
                    pe.wait_ge(hot_out, BATCH * (b - 1))
                for c in range(half * CH // 2, (half + 1) * CH // 2):
                    u = CH * b + c
                    pe.wait_ge(onehot_done, u + 1)
                    for j, k in enumerate(BATCHES[b]):
                        if c % (CH // 2) == 0:
                            pe.wait_ge(hi_done, pieces(k, c))
                            pe.wait_ge(lo_done, pieces(k, c))
                        cols = onehot[0:HR, u % RING, j * B:(j + 1) * B]
                        bank = (BATCH * b + j) % 4
                        pe.matmul(ps[:, bank, :], hi[0:HR, k % SPLITS, c, :], cols,
                                  start=(c == 0), stop=False)
                        mm = pe.matmul(ps[:, bank, :], lo[0:HR, k % SPLITS, c, :], cols,
                                       start=False, stop=(c == CH - 1))
                    mm.then_inc(onehot_used, 1)

            def turn(t, g):
                i = turns.index((t, g))
                pe.wait_ge(gathered[t, g], 16 * len(GG[g]))
                if i == 0:
                    pe.wait_ge(dense_out, 1)
                else:
                    pe.wait_ge(turn_out, i)
                for q, slot in enumerate(GG[g]):
                    mm = pe.transpose(ps[:, TURN, q * P:(q + 1) * P],
                                      E[:, t % 2, GAT_F.index(ORDER[slot]), :], ident)
                mm.then_inc(turn_done, 1)

            def window(t, w):
                i = dots.index((t, w))
                if w == 0:
                    pe.wait_ge(turn_out, turns.index((t, len(GG) - 1)) + 1)
                    if t == 0:
                        pe.wait_ge(pads_set, 1)
                        pe.wait_ge(hot_out, HOT)
                if i >= 2:
                    pe.wait_ge(dots_out, i - 1)
                for g in range(WG[w]):
                    c0 = t * P + 4 * (sum(WG[:w]) + g)
                    at = (g % 4) * PITCH
                    mm = pe.matmul(ps[:, 3 * (i % 2) + g // 4, at:at + 4 * F],
                                   eT[:, c0:c0 + 4, :].rearrange("p s f -> p (s f)"),
                                   eT[:, c0:c0 + 4, 0:F], start=True, stop=True)
                mm.then_inc(dots_done, 1)

            def layer1(t):
                if t == 0:
                    pe.wait_ge(w_in, 96)
                elif t < T - 1:
                    pe.wait_ge(l3_out, t)
                pe.wait_ge(dots_out, dots.index((t, W - 1)) + 1)
                for n in range(N1):
                    for k in range(KT):
                        r = P if k < KT - 1 else 96 + DENSE
                        mm = pe.matmul(ps[:, l1_bank(t, n), n * P:(n + 1) * P],
                                       w1_sb[0:r, k, n * P:(n + 1) * P], G[0:r, t, k, :],
                                       start=(k == 0), stop=(k == KT - 1))
                    if n % 2:
                        mm.then_inc(l1_done, 1)

            def layer2(t):
                if t == T - 1:
                    pe.wait_ge(turn_out, len(turns))
                for k in range(N1):
                    if t < T - 1:
                        pe.wait_ge(l1_out_s, N1 * (t + 1))
                    elif k < 2:
                        pe.wait_ge(l1_out_s, N1 * t + k + 1)
                    else:
                        pe.wait_ge(l1_out_v, 1)
                    for n in range(N2):
                        mm = pe.matmul(ps[:, l2_bank(t, n), n * P:(n + 1) * P],
                                       w2_sb[:, k, n * P:(n + 1) * P], h1[:, t % 2, k, :],
                                       start=(k == 0 and (n == 0 or t == T - 1)), stop=(k == N1 - 1),
                                       skip_group_check=True)
                mm.then_inc(l2_done, 1)

            def layer3(t):
                pe.wait_ge(l2_out_s, t + 1)
                if t == T - 1:
                    pe.wait_ge(l2_out_v, 1)
                for k in range(N2):
                    mm = pe.matmul(ps[:, l3_bank(t), 0:1], h2[:, t % 2, k, :],
                                   wb[:, N1 + N2 + k:N1 + N2 + k + 1], start=(k == 0), stop=(k == N2 - 1))
                mm.then_inc(l3_done, 1)

            pe.wait_ge(warm_set, 1)
            for _ in range(WARM):
                pe.matmul(ps[:, MLP, :], warm[:, 0:P], warm[:, :], start=True, stop=True)
            pe.wait_ge(const_in, 16)
            for n, (kind, a, b) in enumerate(steps):
                if kind == "hot":
                    hot(a, b)
                elif kind == "turn":
                    turn(a, b)
                elif kind == "dots":
                    window(a, b)
                elif kind == "l1":
                    layer1(a)
                elif kind == "l2":
                    layer2(a)
                else:
                    layer3(a)
                if n == 0:
                    pe.wait_ge(dense_in, 16)
                    for t in range(T):
                        mm = pe.transpose(ps[0:DENSE, TURN, t * P:(t + 1) * P], dn[:, t, :], ident)
                    mm.then_inc(dense_turned, 1)

        @block.vector
        def _(dve):
            def low(k, c0, c1):
                dve.wait_ge(hi_done, pieces(k, c0))
                if k >= SPLITS:
                    dve.wait_ge(onehot_used, CH * ((k - SPLITS) // BATCH + 1))
                dve.tensor_tensor(lo[0:HR, k % SPLITS, c0:c1, :], raw[0:HR, k % RAWS, c0:c1, :],
                                  hi[0:HR, k % SPLITS, c0:c1, :].bitcast(F32), ALU.subtract
                                  ).then_inc(lo_done, 1)

            def columns(b, c):
                u, n = CH * b + c, len(BATCHES[b]) * B
                if c == 0:
                    dve.wait_ge(idsb_in[b], 16)
                if u >= RING:
                    dve.wait_ge(onehot_used, u - RING + 1)
                dve.tensor_scalar(onehot[0:HR, u % RING, 0:n], idsb[0:HR, b % 2, 0:n],
                                  csb[0:HR, P + c:P + c + 1], None, ALU.is_equal
                                  ).then_inc(onehot_done, 1)

            dve.memset(eT[:, :, F:SLOTS], 0.0).then_inc(pads_set, 1)
            dve.wait_ge(const_in, 16)
            for b in range(len(BATCHES)):
                mine = loads(0) if b == 0 else []
                following = loads(b + 1) if b + 1 < len(BATCHES) else []
                for c in range(CH):
                    columns(b, c)
                    while mine and c in (0, 3) and len(mine) > (len(loads(0)) // 2 if c == 0 else 0):
                        low(*mine.pop(0))
                    if following and c in (5, 7):
                        low(*following.pop(0))
            dve.wait_ge(w_in, 96)
            for i, (t, w) in enumerate(dots):
                for s in range(4):
                    dve.wait_ge(base_out, 4 * i + s + 1)
                    for m in range(4):
                        src, cols, ng = own(i, s, m, KT - 1)
                        op = dve.copy_predicated(
                            G[32 * m:32 * m + 32, t, 0:KT - 1, cols],
                            mask[32 * m:32 * m + 32, :].unsqueeze(2).to_broadcast([32, KT - 1, ng]), src)
                op.then_inc(dots_out, 1)
            dve.wait_ge(l1_done, 2 * T)
            for k in (2, 3):
                op = dve.tensor_scalar(h1[:, (T - 1) % 2, k, :], ps[:, l1_bank(T - 1, k), k * P:(k + 1) * P],
                                       wb[:, k:k + 1], 0.0, ALU.add, ALU.max)
            op.then_inc(l1_out_v, 1)
            dve.wait_ge(l2_done, T)
            dve.tensor_scalar(h2[:, (T - 1) % 2, 1, :], ps[:, l2_bank(T - 1, 1), P:2 * P], wb[:, N1 + 1:N1 + 2], 0.0,
                              ALU.add, ALU.max).then_inc(l2_out_v, 1)

        @block.scalar
        def _(act):
            def high(i, k, c0, c1):
                act.wait_ge(piece_in[i], 16)
                if k >= SPLITS:
                    act.wait_ge(onehot_used, CH * ((k - SPLITS) // BATCH + 1))
                act.copy(hi[0:HR, k % SPLITS, c0:c1, :], raw[0:HR, k % RAWS, c0:c1, :]).then_inc(hi_done, 1)

            following = list(enumerate(x for b in range(len(BATCHES)) for x in loads(b)))
            for _ in loads(0) + loads(1):
                i, x = following.pop(0)
                high(i, *x)
            act.wait_ge(dense_turned, 1)
            act.copy(G[96:96 + DENSE, :, KT - 1, :],
                     ps[0:DENSE, TURN, :].rearrange("p (t b) -> p t b", t=T)).then_inc(dense_out, 1)
            for n, (kind, a, b) in enumerate(steps):
                if kind == "hot":
                    if b == 1:
                        act.wait_ge(onehot_used, CH * (a + 1))
                    if following and (b == 1 or a > 0):
                        i, x = following.pop(0)
                        high(i, *x)
                    if b == 1:
                        for j, k in enumerate(BATCHES[a]):
                            act.copy(eT[:, :, NG + k], ps[:, (BATCH * a + j) % 4, :]).then_inc(hot_out, 1)
                elif kind == "turn":
                    s0, ns = GG[b][0], len(GG[b])
                    act.wait_ge(turn_done, turns.index((a, b)) + 1)
                    act.copy(eT[:, a * P:(a + 1) * P, s0:s0 + ns],
                             ps[:, TURN, 0:ns * P].rearrange("p (f b) -> p b f", f=ns)).then_inc(turn_out, 1)
                elif kind == "dots":
                    i = dots.index((a, b))
                    act.wait_ge(dots_done, i + 1)
                    for s in range(4):
                        for m in range(4):
                            src, cols, _ = own(i, s, PAIRED // 2 + m, KT if m < SINGLE else KT - 1)
                            op = act.copy(G[32 * m:32 * m + 32, a, 0:src.shape[1], cols], src)
                        op.then_inc(base_out, 1)
                elif kind == "l1":
                    act.wait_ge(l1_done, 2 * (a + 1) if a < T - 1 else 2 * a + 1)
                    for k in range(N1 if a < T - 1 else 2):
                        act.activation(h1[:, a % 2, k, :], ps[:, l1_bank(a, k), k * P:(k + 1) * P], ACT.Relu,
                                       bias=wb[:, k:k + 1]).then_inc(l1_out_s, 1)
                elif kind == "l2":
                    act.wait_ge(l2_done, a + 1)
                    for k in range(N2 if a < T - 1 else 1):
                        op = act.activation(h2[:, a % 2, k, :], ps[:, l2_bank(a, k), k * P:(k + 1) * P],
                                            ACT.Relu, bias=wb[:, N1 + k:N1 + k + 1])
                    op.then_inc(l2_out_s, 1)
                else:
                    act.wait_ge(l3_done, a + 1)
                    act.copy(y[:, a:a + 1], ps[:, l3_bank(a), 0:1]).then_inc(l3_out, 1)


def first_layer_rows():
    rows = np.full((P, KT), -1)

    def put(column, slot, m, k):
        a, b = sorted((ORDER[column], ORDER[slot]))
        rows[32 * m + slot, k] = b * (b - 1) // 2 + a

    half = PAIRED // 2
    for c in range(half):
        m, k = c % 4, c // 4
        for d in range(1, half + 1):
            put(c, (c + d) % PAIRED, m, k)
        for d in range(1, half):
            put(c + half, (c + half + d) % PAIRED, m, k)
    for m in range(SINGLE):
        for slot in range(PAIRED + m):
            put(PAIRED + m, slot, m, KT - 1)
    for d in range(DENSE):
        rows[96 + d, KT - 1] = F * (F - 1) // 2 + d
    assert sorted(rows[rows >= 0]) == list(range(F * (F - 1) // 2 + DENSE))
    return rows


def column_mask():
    mask = np.zeros((P, KT - 1), np.int32)
    for c in range(PAIRED // 2):
        mask[32 * (c % 4) + c + 1:32 * (c % 4) + c + PAIRED // 2 + 1, c // 4] = 1
    return mask


def kernel(**inputs):
    import concourse.bacc as bacc
    from concourse.bass_utils import run_bass_kernel_spmd

    W1 = np.asarray(inputs["W_top1"])
    rows = first_layer_rows()
    w1 = np.zeros((P, KT, H1), W1.dtype)
    w1[rows >= 0] = W1[rows[rows >= 0]]
    ids = np.asarray(inputs["ids"])
    consts = np.concatenate([np.eye(P), CH * np.arange(P)[:, None] + np.arange(CH)], 1).astype(np.float32)
    arrays = {
        "ids": ids.reshape(P, T * F),
        "ids_hot": ids.reshape(P, T, F)[:, :, HOT_F].transpose(2, 1, 0).reshape(1, HOT * B),
        "dense": inputs["dense_ctx"],
        "w1": w1,
        "b1": np.asarray(inputs["b_top1"]).reshape(N1, P).T,
        "w2": inputs["W_top2"],
        "b2": np.asarray(inputs["b_top2"]).reshape(N2, P).T,
        "w3": np.asarray(inputs["W_top3"]).reshape(N2, P).T,
        "consts": consts,
        "mask": column_mask(),
    }
    for f in range(F):
        arrays[f"tbl_{f}"] = inputs[f"tbl_{f}"]
    nc = bacc.Bacc("TRN2", target_bir_lowering=False, num_devices=1)
    aps = {}
    for name in arrays:
        a = arrays[name] = np.ascontiguousarray(arrays[name])
        aps[name] = nc.dram_tensor(f"in_{name}", a.shape, mybir.dt.from_np(a.dtype), kind="ExternalInput").ap()
    out = nc.dram_tensor("out", (B, 1), F32, kind="ExternalOutput").ap()
    build(nc, aps["ids"], aps["ids_hot"], aps["dense"], [aps[f"tbl_{f}"] for f in range(F)], aps["w1"],
          aps["b1"], aps["w2"], aps["b2"], aps["w3"], aps["consts"], aps["mask"], out)
    r = run_bass_kernel_spmd(nc, [{f"in_{n}": a for n, a in arrays.items()}], core_ids=[0])
    return r.results[0]["out"]
```

```python
from contextlib import ExitStack

import numpy as np

import concourse.bass as bass
from concourse import mybir

P = 128
T = 4
B = T * P
F = 27
PAIRED = 24
SLOTS = 32
DENSE = 16
H1, H2 = 512, 256
HOT = 9
WHOLE = 8
FIRST = 1
CH = 8
HR = 125
BATCH = 2
RING = 5
WARM = 4
RAWS = 4
SPLITS = 2 * BATCH
PER = 4
WG = [[8, 8, 8, 8]] * (T - 1) + [[8, 12, 12]]
TURNS = 2
PITCH = 128
KT = 3
EXTRA = 2
N1, N2 = H1 // P, H2 // P

V = [125000, 1000, 12500, 12500, 1250, 12500, 12500, 12500, 1250, 12500, 12500, 12500, 1000,
     1000, 1250, 1000, 12500, 1000, 1250, 1000, 1000, 1000, 1000, 1000, 1000, 1000, 1000]
HOT_F = [f for f in range(F) if V[f] == CH * HR][:HOT]
GAT_F = [f for f in range(F) if f not in HOT_F]
SINGLE = F - PAIRED
ORDER = GAT_F + HOT_F[WHOLE:] + HOT_F[SINGLE:WHOLE] + HOT_F[:SINGLE]
NG = [len(GAT_F) + (HOT - WHOLE if t < FIRST else 0) for t in range(T)]
GG = [[list(range(a, min(a + PER, n))) for a in range(0, n, PER)] for n in NG]
BATCHES = [(list(range(a, min(a + BATCH, WHOLE))), 0, B) for a in range(0, WHOLE, BATCH)] + [
    ([k], FIRST * P, B) for k in range(WHOLE, HOT)]

F32 = mybir.dt.float32
F32R = mybir.dt.float32r
I32 = mybir.dt.int32
U32 = mybir.dt.uint32
ALU = mybir.AluOpType
ACT = mybir.ActivationFunctionType


def parts(k):
    return [(0, CH // 2), (CH // 2, CH)] if k < BATCH else [(0, CH)]


def pieces(k, c):
    if k < BATCH:
        return (c // (CH // 2)) * BATCH + k + 1
    return BATCH + k + 1


def loads(b):
    new = [k for k in BATCHES[b][0] if all(k not in x[0] for x in BATCHES[:b])]
    return [(k,) + parts(k)[i] for i in range(len(parts(new[0]) if new else [])) for k in new]


def onehot_place(b, c):
    serial, n = [], 0
    for x in range(b + 1):
        share = 1 if x < WHOLE // BATCH else 2
        serial += [n + y // share for y in range(CH)]
        n = serial[-1] + 1
    v = serial[CH * b + c]
    before = [i for i, w in enumerate(serial) if w == v - RING]
    share = 1 if b < WHOLE // BATCH else 2
    return v % RING, (c % share) * B, before[-1] + 1 if before else 0


def outputs(t):
    last = max(b for b, (_, s0, s1) in enumerate(BATCHES) if s0 <= t * P < s1)
    return sum(len(x[0]) for x in BATCHES[:last + 1])


STEPS = """
    hot 0 0, hot 0 1, turn 0 0, hot 1 0, turn 0 1, dense, hot 1 1, turn 0 2, hot 2 0, turn 0 3,
    hot 2 1, turn 0 4, turn 1 0, hot 3 0, turn 1 1, hot 3 1, turn 1 2, hot 4 0,
    dots 0 0, turn 1 3, dots 0 1, hot 4 1, dots 0 2, turn 1 4, dots 0 3, turn 2 0,
    dots 1 0, turn 2 1, dots 1 1, l1 0,
    dots 1 2, turn 2 2, dots 1 3, turn 2 3, turn 2 4, l2 0, dots 2 0, l3 0, dots 2 1,
    turn 3 0, l1 1, dots 2 2, dots 2 3, turn 3 1, turn 3 2, l2 1,
    l1 2, turn 3 3, turn 3 4, l3 1, dots 3 0, dots 3 1, dots 3 2, l2 2, l1 3, l3 2, l2 3, l3 3"""
STEPS = [(x.split()[0], *map(int, x.split()[1:])) for x in STEPS.split(",")]


def build(nc, ids, ids_hot, dense, tables, w1, w1_dense, b1, w2, b2, w3, consts, take_c, out):
    turns = [x[1:] for x in STEPS if x[0] == "turn"]
    dots = [x[1:] for x in STEPS if x[0] == "dots"]

    with ExitStack() as ctx:
        def sb(name, shape, dt=F32):
            return ctx.enter_context(nc.sbuf_tensor(name, shape, dt))

        def sem(name):
            return ctx.enter_context(nc.semaphore(name))

        ids_sb = sb("ids_sb", [P, T * F], I32)
        csb = sb("csb", [P, P + CH])
        mask = sb("mask", [P, KT + EXTRA], I32)
        warm = sb("warm", [P, 512])
        idsb = sb("idsb", [P, 2, BATCH * B], I32)
        raw = sb("raw", [P, RAWS, CH, P])
        hi = sb("hi", [P, SPLITS, CH, P], F32R)
        lo = sb("lo", [P, SPLITS, CH, P], F32R)
        onehot = sb("onehot", [P, RING, BATCH * B], F32R)
        E = sb("E", [P, 2, max(NG), P])
        eT = sb("eT", [P, B, SLOTS])
        G = sb("G", [P, T, KT, P])
        w1_sb = sb("w1_sb", [P, KT, H1])
        w1d = sb("w1d", [P, H1])
        w1d_parts = sb("w1d_parts", [P, H1], F32R)
        dense_parts = sb("dense_parts", [P, T, P], F32R)
        w2_sb = sb("w2_sb", [P, N1, H2])
        wb = sb("wb", [P, N1 + 2 * N2])
        dn = sb("dn", [P, T, DENSE])
        dn4 = sb("dn4", [P, T, 4, 32])
        h1 = sb("h1", [P, 2, N1, P])
        h2 = sb("h2", [P, 2, N2, P])
        y = sb("y", [P, T])
        ident = csb[:, 0:P]
        ps = ctx.enter_context(nc.psum_tensor("ps", [P, 8, 512], F32))
        TURN, MLP = 4, 6

        ids_in, const_in, dense_in, w_in = sem("ids_in"), sem("const_in"), sem("dense_in"), sem("w_in")
        w1d_in = sem("w1d_in")
        idsb_in = [sem(f"idsb_in{b}") for b in range(len(BATCHES))]
        piece_in = [sem(f"piece_in{i}") for i in range(sum(len(loads(b)) for b in range(len(BATCHES))))]
        gathered = {(t, g): sem(f"gathered{t}_{g}") for t in range(T) for g in range(len(GG[t]))}
        warm_set = sem("warm_set")
        hi_done, lo_done = sem("hi_done"), sem("lo_done")
        onehot_done, onehot_used, hot_out = sem("onehot_done"), sem("onehot_used"), sem("hot_out")
        turn_done, turn_out = sem("turn_done"), sem("turn_out")
        last_turn_out = sem("last_turn_out")
        dn4_zero, dense_set, dense_turned = sem("dn4_zero"), sem("dense_set"), sem("dense_turned")
        dense_hi, dense_lo, w1d_hi, w1d_lo = sem("dense_hi"), sem("dense_lo"), sem("w1d_hi"), sem("w1d_lo")
        dots_done, base_out = sem("dots_done"), sem("base_out")
        over_done, dots_out = sem("over_done"), sem("dots_out")
        l1_done, l1_out_s, l1_out_v = sem("l1_done"), sem("l1_out_s"), sem("l1_out_v")
        l2_done, l2_out_s, l2_out_v = sem("l2_done"), sem("l2_out_s"), sem("l2_out_v")
        l3_done, l3_out, stored = sem("l3_done"), sem("l3_out"), sem("stored")
        block = ctx.enter_context(nc.Block())

        def window_bank(t, w):
            return (3 if t == T - 1 else 2) * (w % 2)

        def own(i, s, first, k, step=4):
            t, w = dots[i]
            bank = window_bank(t, w)
            ng, g0 = WG[t][w], sum(WG[t][:w])
            src = ps[32 * s:32 * s + 32, bank:bank + ng // 4, :].rearrange("p k c -> p (k c)")
            src = src[:, 0:ng * PITCH].rearrange("p (g c) -> p g c", c=PITCH)
            a = s * F + first
            src = src[:, :, a:a + step * (k - 1) + 1:step].rearrange("p g k -> p k g")
            return src, slice(4 * g0 + s, 4 * (g0 + ng), 4), ng

        def hot_bank(b, j):
            return MLP + 1 if b == len(BATCHES) - 1 else (BATCH * b + j) % 4

        def l1_bank(t, n):
            return {T - 2: 2, T - 1: 3}.get(t, MLP) + n // 2

        def l2_bank(t, n):
            return (0 if t == T - 1 else MLP) + n

        def l3_bank(t):
            return 5 if t == T - 1 else MLP

        @block.sync
        def _(sp):
            sp.dma_start(ids_sb[:, :], ids).then_inc(ids_in, 16)
            i = 0
            for b, (ks, s0, s1) in enumerate(BATCHES):
                def ids_of_batch():
                    if b >= 2:
                        sp.wait_ge(onehot_done, CH * (b - 1))
                    a0, a1 = ks[0] * B + s0, ks[-1] * B + s1
                    sp.dma_start(idsb[0:HR, b % 2, 0:a1 - a0],
                                 ids_hot[:, a0:a1].to_broadcast([HR, a1 - a0])).then_inc(idsb_in[b], 16)

                if b == 1:
                    ids_of_batch()
                for k, c0, c1 in loads(b):
                    if k >= RAWS:
                        sp.wait_ge(lo_done, pieces(k - RAWS, CH - 1))
                    sp.dma_start(raw[0:HR, k % RAWS, c0:c1, :],
                                 tables[HOT_F[k]].rearrange("(p c) d -> p c d", c=CH)[:, c0:c1, :]
                                 ).then_inc(piece_in[i], 16)
                    i += 1
                    if i == 1:
                        ids_of_batch()
                        sp.dma_start(csb[:, :], consts).then_inc(const_in, 16)
                if b == 1:
                    sp.dma_start(dn[:, :, :], dense.rearrange("(p t) f -> p t f", t=T)).then_inc(dense_in, 16)
                if b >= 2:
                    ids_of_batch()
                if b == 2:
                    sp.dma_start(w1_sb[:, :, :], w1).then_inc(w_in, 16)
                    sp.dma_start(w1d[:, :], w1_dense).then_inc(w1d_in, 16)
                    sp.dma_start(w2_sb[:, :, :], w2.rearrange("(k p) n -> p k n", p=P)).then_inc(w_in, 16)
                    sp.dma_start(wb[:, 0:N1], b1).then_inc(w_in, 16)
                    sp.dma_start(wb[:, N1:N1 + N2], b2).then_inc(w_in, 16)
                    sp.dma_start(wb[:, N1 + N2:], w3).then_inc(w_in, 16)
                    sp.dma_start(mask[:, :], take_c).then_inc(w_in, 16)
            sp.wait_ge(l3_out, T)
            sp.dma_start(out.rearrange("(p t) f -> p (t f)", t=T), y[:, :]).then_inc(stored, 16)
            sp.wait_ge(stored, 16)

        @block.gpsimd
        def _(pool):
            pool.memset(warm[:, :], 0.0).then_inc(warm_set, 1)
            pool.wait_ge(ids_in, 16)
            for t in range(T):
                for g, slots in enumerate(GG[t]):
                    if t >= 2:
                        pool.wait_ge(turn_done, turns.index((t - 2, g)) + 1)
                    for slot in slots:
                        f = ORDER[slot]
                        pool.indirect_dma_start(
                            out=E[:, t % 2, slot, :], out_offset=None, in_=tables[f],
                            in_offset=bass.IndirectOffsetOnAxis(
                                ap=ids_sb[:, t * F + f:t * F + f + 1].bitcast(U32), axis=0),
                        ).then_inc(gathered[t, g], 16)

        @block.tensor
        def _(pe):
            def hot(b, half):
                if half == 0 and b >= 2:
                    pe.wait_ge(hot_out, BATCH * (b - 1))
                for c in range(half * CH // 2, (half + 1) * CH // 2):
                    u = CH * b + c
                    pe.wait_ge(onehot_done, u + 1)
                    ks, s0, s1 = BATCHES[b]
                    buffer, col, _ = onehot_place(b, c)
                    for j, k in enumerate(ks):
                        if c % (CH // 2) == 0:
                            pe.wait_ge(hi_done, pieces(k, c))
                            pe.wait_ge(lo_done, pieces(k, c))
                        cols = onehot[0:HR, buffer, col + j * (s1 - s0):col + (j + 1) * (s1 - s0)]
                        acc = ps[:, hot_bank(b, j), 0:s1 - s0]
                        pe.matmul(acc, hi[0:HR, k % SPLITS, c, :], cols,
                                  start=(c == 0), stop=False)
                        mm = pe.matmul(acc, lo[0:HR, k % SPLITS, c, :], cols,
                                       start=False, stop=(c == CH - 1))
                    mm.then_inc(onehot_used, 1)

            def turn_dense():
                pe.wait_ge(dense_set, 1)
                for t in range(T):
                    mm = pe.transpose(ps[:, MLP, t * P:(t + 1) * P],
                                      dn4[:, t, :, :].rearrange("p q f -> p (q f)"), ident)
                mm.then_inc(dense_turned, 1)

            def turn(t, g):
                i = turns.index((t, g))
                pe.wait_ge(gathered[t, g], 16 * len(GG[t][g]))
                if i >= TURNS:
                    pe.wait_ge(turn_out, i - TURNS + 1)
                for q, slot in enumerate(GG[t][g]):
                    mm = pe.transpose(ps[:, TURN + i % TURNS, q * P:(q + 1) * P],
                                      E[:, t % 2, slot, :], ident)
                mm.then_inc(turn_done, 1)

            def window(t, w):
                i = dots.index((t, w))
                if w == 0:
                    if t == T - 1:
                        pe.wait_ge(turn_out, len(turns) - 1)
                        pe.wait_ge(last_turn_out, 1)
                    else:
                        pe.wait_ge(turn_out, turns.index((t, len(GG[t]) - 1)) + 1)
                    if t in (0, FIRST):
                        pe.wait_ge(hot_out, outputs(t))
                if i >= 2:
                    pe.wait_ge(dots_out, i if (t, w) == (T - 1, 0) else i - 1)
                if (t, w) == (T - 1, 1):
                    pe.wait_ge(l1_out_s, N1 * t)
                for g in range(WG[t][w]):
                    c0 = t * P + 4 * (sum(WG[t][:w]) + g)
                    at = (g % 4) * PITCH
                    mm = pe.matmul(ps[:, window_bank(t, w) + g // 4, at:at + 4 * F],
                                   eT[:, c0:c0 + 4, :].rearrange("p s f -> p (s f)"),
                                   eT[:, c0:c0 + 4, 0:F], start=True, stop=True)
                mm.then_inc(dots_done, 1)

            def layer1(t):
                if t == 0:
                    pe.wait_ge(hot_out, outputs(T - 1))
                    pe.wait_ge(w_in, 96)
                    pe.wait_ge(w1d_lo, 2)
                    pe.wait_ge(dense_lo, 1)
                elif t < T - 2:
                    pe.wait_ge(l3_out, t)
                else:
                    pe.wait_ge(dots_out, dots.index((t, len(WG[t]) - 1 if t == T - 2 else 1)) + 1)
                for n in range(N1):
                    pe.matmul(ps[:, l1_bank(t, n), n * P:(n + 1) * P],
                              w1d_parts[:, n * P:(n + 1) * P], dense_parts[:, t, :],
                              start=(n % 2 == 0), stop=False, skip_group_check=True)
                pe.wait_ge(dots_out, dots.index((t, len(WG[t]) - 1)) + 1)
                for n in range(N1):
                    for k in range(KT):
                        mm = pe.matmul(ps[:, l1_bank(t, n), n * P:(n + 1) * P],
                                       w1_sb[:, k, n * P:(n + 1) * P], G[:, t, k, :],
                                       start=False, stop=(k == KT - 1), skip_group_check=True)
                    if n % 2:
                        mm.then_inc(l1_done, 1)

            def layer2(t):
                if t == T - 2:
                    pe.wait_ge(l3_out, t)
                for k in range(N1):
                    if t < T - 1:
                        pe.wait_ge(l1_out_s, N1 * (t + 1))
                    elif k < 2:
                        pe.wait_ge(l1_out_s, N1 * t + k + 1)
                    else:
                        pe.wait_ge(l1_out_v, 1)
                    for n in range(N2):
                        mm = pe.matmul(ps[:, l2_bank(t, n), n * P:(n + 1) * P],
                                       w2_sb[:, k, n * P:(n + 1) * P], h1[:, t % 2, k, :],
                                       start=(k == 0), stop=(k == N1 - 1),
                                       skip_group_check=True)
                mm.then_inc(l2_done, 1)

            def layer3(t):
                pe.wait_ge(l2_out_s, t + 1)
                if t == T - 1:
                    pe.wait_ge(l2_out_v, 1)
                for k in range(N2):
                    mm = pe.matmul(ps[:, l3_bank(t), 0:1], h2[:, t % 2, k, :],
                                   wb[:, N1 + N2 + k:N1 + N2 + k + 1], start=(k == 0), stop=(k == N2 - 1))
                mm.then_inc(l3_done, 1)

            pe.wait_ge(warm_set, 1)
            for _ in range(WARM):
                pe.matmul(ps[:, MLP, :], warm[:, 0:P], warm[:, :], start=True, stop=True)
            pe.wait_ge(const_in, 16)
            for kind, *x in STEPS:
                if kind == "hot":
                    hot(*x)
                elif kind == "dense":
                    turn_dense()
                elif kind == "turn":
                    turn(*x)
                elif kind == "dots":
                    window(*x)
                elif kind == "l1":
                    layer1(*x)
                elif kind == "l2":
                    layer2(*x)
                else:
                    layer3(*x)

        @block.vector
        def _(dve):
            def low(k, c0, c1):
                dve.wait_ge(hi_done, pieces(k, c0))
                if k >= SPLITS:
                    dve.wait_ge(onehot_used, CH * ((k - SPLITS) // BATCH + 1))
                dve.tensor_tensor(lo[0:HR, k % SPLITS, c0:c1, :], raw[0:HR, k % RAWS, c0:c1, :],
                                  hi[0:HR, k % SPLITS, c0:c1, :].bitcast(F32), ALU.subtract
                                  ).then_inc(lo_done, 1)

            def columns(b, c):
                ks, s0, s1 = BATCHES[b]
                n = len(ks) * (s1 - s0)
                buffer, col, used = onehot_place(b, c)
                if c == 0:
                    dve.wait_ge(idsb_in[b], 16)
                if used:
                    dve.wait_ge(onehot_used, used)
                dve.tensor_scalar(onehot[0:HR, buffer, col:col + n], idsb[0:HR, b % 2, 0:n],
                                  csb[0:HR, P + c:P + c + 1], None, ALU.is_equal
                                  ).then_inc(onehot_done, 1)

            dve.memset(dn4[:, :, :, :], 0.0).then_inc(dn4_zero, 1)
            dve.wait_ge(const_in, 16)
            for b in range(len(BATCHES)):
                mine = loads(0) if b == 0 else []
                following = loads(b + 1) if b + 1 < len(BATCHES) else []
                for c in range(CH):
                    columns(b, c)
                    while mine and c in (0, 3) and len(mine) > (len(loads(0)) // 2 if c == 0 else 0):
                        low(*mine.pop(0))
                    if following and c in (5, 7):
                        low(*following.pop(0))
                    if b == 1 and c == 1:
                        dve.wait_ge(dense_in, 16)
                        dve.wait_ge(dn4_zero, 1)
                        dve.tensor_copy(dn4[:, :, :, 0:DENSE],
                                        dn[:, :, :].unsqueeze(2).to_broadcast([P, T, 4, DENSE])
                                        ).then_inc(dense_set, 1)
                    if b == 2 and c == 1:
                        dve.wait_ge(dense_hi, 1)
                        dve.tensor_tensor(dense_parts[64:P, :, :],
                                          ps[64:P, MLP, :].rearrange("p (t b) -> p t b", t=T),
                                          dense_parts[64:P, :, :].bitcast(F32), ALU.subtract
                                          ).then_inc(dense_lo, 1)
            dve.wait_ge(w1d_hi, 1)
            for q in (1, 3):
                rows = slice(32 * q, 32 * q + 32)
                dve.tensor_tensor(w1d_parts[rows, :], w1d[rows, :], w1d_parts[rows, :].bitcast(F32),
                                  ALU.subtract).then_inc(w1d_lo, 1)
            dve.wait_ge(w_in, 96)
            for i, (t, w) in enumerate(dots):
                if (t, w) == (T - 1, 0):
                    dve.wait_ge(turn_done, len(turns))
                    s0, ns, bank = GG[t][-1][0], len(GG[t][-1]), TURN + (len(turns) - 1) % TURNS
                    dve.tensor_copy(eT[:, t * P:(t + 1) * P, s0:s0 + ns],
                                    ps[:, bank, 0:ns * P].rearrange("p (f b) -> p b f", f=ns)
                                    ).then_inc(last_turn_out, 1)
                for s in range(4):
                    dve.wait_ge(base_out, 4 * i + s + 1)
                    for m in range(4):
                        src, cols, ng = own(i, s, m, KT)
                        op = dve.copy_predicated(
                            G[32 * m:32 * m + 32, t, :, cols],
                            mask[32 * m:32 * m + 32, 0:KT].unsqueeze(2).to_broadcast([32, KT, ng]), src)
                        if m == 0:
                            op.then_inc(over_done, 1)
                    src, cols, ng = own(i, s, F - EXTRA, EXTRA, step=1)
                    dve.wait_ge(over_done, 4 * i + s + 1)
                    op = dve.copy_predicated(G[0:32, t, 0:EXTRA, cols],
                                             mask[0:32, KT:].unsqueeze(2).to_broadcast([32, EXTRA, ng]), src)
                op.then_inc(dots_out, 1)
            dve.wait_ge(l1_done, 2 * T)
            for k in (2, 3):
                op = dve.tensor_scalar(h1[:, (T - 1) % 2, k, :], ps[:, l1_bank(T - 1, k), k * P:(k + 1) * P],
                                       wb[:, k:k + 1], 0.0, ALU.add, ALU.max)
            op.then_inc(l1_out_v, 1)
            dve.wait_ge(l2_done, T)
            dve.tensor_scalar(h2[:, (T - 1) % 2, 1, :], ps[:, l2_bank(T - 1, 1), P:2 * P], wb[:, N1 + 1:N1 + 2], 0.0,
                              ALU.add, ALU.max).then_inc(l2_out_v, 1)

        @block.scalar
        def _(act):
            def high(i, k, c0, c1):
                act.wait_ge(piece_in[i], 16)
                if k >= SPLITS:
                    act.wait_ge(onehot_used, CH * ((k - SPLITS) // BATCH + 1))
                act.copy(hi[0:HR, k % SPLITS, c0:c1, :], raw[0:HR, k % RAWS, c0:c1, :]).then_inc(hi_done, 1)

            following = list(enumerate(x for b in range(len(BATCHES)) for x in loads(b)))
            for _ in loads(0) + loads(1):
                i, x = following.pop(0)
                high(i, *x)
            for kind, a, b in ((*x, 0, 0)[:3] for x in STEPS):
                if kind == "dense":
                    act.wait_ge(dense_turned, 1)
                    act.copy(dense_parts[:, :, :],
                             ps[:, MLP, :].rearrange("p (t b) -> p t b", t=T)).then_inc(dense_hi, 1)
                if (kind, a, b) == ("hot", len(BATCHES) - 2, 0):
                    act.wait_ge(w1d_in, 16)
                    act.copy(w1d_parts[:, :], w1d[:, :]).then_inc(w1d_hi, 1)
                if kind == "hot":
                    if b == 1:
                        act.wait_ge(onehot_used, CH * (a + 1))
                    if following and (b == 1 or a > 0):
                        i, x = following.pop(0)
                        high(i, *x)
                    if b == 1:
                        ks, s0, s1 = BATCHES[a]
                        for j, k in enumerate(ks):
                            slot = ORDER.index(HOT_F[k])
                            places = eT[:, s0:s1, slot:slot + 1 if slot < PAIRED else SLOTS:SINGLE]
                            act.copy(places, ps[:, hot_bank(a, j), 0:s1 - s0].unsqueeze(2)
                                     .to_broadcast([P, s1 - s0, places.shape[2]])).then_inc(hot_out, 1)
                elif kind == "turn" and (a, b) != turns[-1]:
                    s0, ns = GG[a][b][0], len(GG[a][b])
                    i = turns.index((a, b))
                    act.wait_ge(turn_done, i + 1)
                    act.copy(eT[:, a * P:(a + 1) * P, s0:s0 + ns],
                             ps[:, TURN + i % TURNS, 0:ns * P].rearrange("p (f b) -> p b f", f=ns)).then_inc(turn_out, 1)
                elif kind == "dots":
                    i = dots.index((a, b))
                    act.wait_ge(dots_done, i + 1)
                    for s in range(4):
                        for m in range(4):
                            src, cols, _ = own(i, s, PAIRED // 2 + m, KT)
                            op = act.copy(G[32 * m:32 * m + 32, a, :, cols], src)
                        op.then_inc(base_out, 1)
                elif kind == "l1":
                    for k in range(N1 if a < T - 1 else 2):
                        if k % 2 == 0:
                            act.wait_ge(l1_done, 2 * a + k // 2 + 1)
                        act.activation(h1[:, a % 2, k, :], ps[:, l1_bank(a, k), k * P:(k + 1) * P], ACT.Relu,
                                       bias=wb[:, k:k + 1]).then_inc(l1_out_s, 1)
                elif kind == "l2":
                    act.wait_ge(l2_done, a + 1)
                    for k in range(N2 if a < T - 1 else 1):
                        op = act.activation(h2[:, a % 2, k, :], ps[:, l2_bank(a, k), k * P:(k + 1) * P],
                                            ACT.Relu, bias=wb[:, N1 + k:N1 + k + 1])
                    op.then_inc(l2_out_s, 1)
                elif kind == "l3":
                    act.wait_ge(l3_done, a + 1)
                    act.copy(y[:, a:a + 1], ps[:, l3_bank(a), 0:1]).then_inc(l3_out, 1)


def first_layer_rows():
    rows = np.full((P, KT), -1)

    def put(column, place, m, k):
        slot = place if place < F else PAIRED + (place - PAIRED) % SINGLE
        a, b = sorted((ORDER[column], ORDER[slot]))
        rows[32 * m + place, k] = b * (b - 1) // 2 + a

    half = PAIRED // 2
    for c in range(half):
        m, k = c % 4, c // 4
        for d in range(1, half + 1):
            put(c, (c + d) % PAIRED, m, k)
        for d in range(1, half):
            put(c + half, (c + half + d) % PAIRED, m, k)
        for i in range(SINGLE):
            put(c, PAIRED + i, m, k)
            put(c + half, F + i, m, k)
    put(25, 30, 0, 0)
    put(26, 30, 0, 1)
    put(26, 31, 0, 1)
    assert sorted(rows[rows >= 0]) == list(range(F * (F - 1) // 2))
    return rows


def column_mask():
    mask = np.zeros((P, KT + EXTRA), np.int32)
    for c in range(PAIRED // 2):
        mask[32 * (c % 4) + c + 1:32 * (c % 4) + c + PAIRED // 2 + 1, c // 4] = 1
        mask[32 * (c % 4) + PAIRED:32 * (c % 4) + F, c // 4] = 1
    mask[30, KT:] = 1
    mask[31, KT + 1] = 1
    return mask


def kernel(**inputs):
    import concourse.bacc as bacc
    from concourse.bass_utils import run_bass_kernel_spmd

    W1 = np.asarray(inputs["W_top1"])
    rows = first_layer_rows()
    w1 = np.zeros((P, KT, H1), W1.dtype)
    w1[rows >= 0] = W1[rows[rows >= 0]]
    w1_dense = np.zeros((4, 32, H1), W1.dtype)
    w1_dense[:, 0:DENSE] = W1[F * (F - 1) // 2:]
    ids = np.asarray(inputs["ids"])
    consts = np.concatenate([np.eye(P), CH * np.arange(P)[:, None] + np.arange(CH)], 1).astype(np.float32)
    arrays = {
        "ids": ids.reshape(P, T * F),
        "ids_hot": ids.reshape(P, T, F)[:, :, HOT_F].transpose(2, 1, 0).reshape(1, HOT * B),
        "dense": inputs["dense_ctx"],
        "w1": w1,
        "w1_dense": w1_dense.reshape(P, H1),
        "b1": np.asarray(inputs["b_top1"]).reshape(N1, P).T,
        "w2": inputs["W_top2"],
        "b2": np.asarray(inputs["b_top2"]).reshape(N2, P).T,
        "w3": np.asarray(inputs["W_top3"]).reshape(N2, P).T,
        "consts": consts,
        "mask": column_mask(),
    }
    for f in range(F):
        arrays[f"tbl_{f}"] = inputs[f"tbl_{f}"]
    nc = bacc.Bacc("TRN2", target_bir_lowering=False, num_devices=1)
    aps = {}
    for name in arrays:
        a = arrays[name] = np.ascontiguousarray(arrays[name])
        aps[name] = nc.dram_tensor(f"in_{name}", a.shape, mybir.dt.from_np(a.dtype), kind="ExternalInput").ap()
    out = nc.dram_tensor("out", (B, 1), F32, kind="ExternalOutput").ap()
    build(nc, aps["ids"], aps["ids_hot"], aps["dense"], [aps[f"tbl_{f}"] for f in range(F)], aps["w1"],
          aps["w1_dense"], aps["b1"], aps["w2"], aps["b2"], aps["w3"], aps["consts"], aps["mask"], out)
    r = run_bass_kernel_spmd(nc, [{f"in_{n}": a for n, a in arrays.items()}], core_ids=[0])
    return r.results[0]["out"]
```
